# Optimizing a Trainium2 kernel written in Bass

```python
import numpy as np
import jax
import jax.numpy as jnp

def _softmax(x, axis=-1):
    return jax.nn.softmax(x, axis=axis)

def _gelu(x):
    return jax.nn.gelu(x, approximate=True)

def _silu(x):
    return jax.nn.silu(x)

def _sigmoid(x):
    return jax.nn.sigmoid(x)

def _layernorm(x, axis=-1, eps=1e-05):
    m = jnp.mean(x, axis=axis, keepdims=True)
    v = jnp.var(x, axis=axis, keepdims=True)
    return (x - m) / jnp.sqrt(v + eps)

def _scatter_add(tgt, idx, src, axis=0):
    return tgt.at[idx].add(src)

def _segment_sum(src, seg, n):
    return jax.ops.segment_sum(src, seg, n)
kernel_name = 'mk_adj_seq_d1_adj_r2_ac45ef'

def setup_inputs(seed: int=0):
    np.random.seed(seed)
    _w = jnp.asarray

    def _rec_inputs():
        import jax
        import jax.numpy as jnp
        _gk = jax.random.key(seed)
        x = -0.0005207 + 1.001 * jax.random.normal(jax.random.fold_in(_gk, 1), (8, 2048, 128), jnp.float32)
        _w = (1.0 + jnp.arange(2048, dtype=jnp.float32)) ** (-0.5)
        _w = _w / _w.mean()
        _pij = jnp.clip(0.000976562 * _w[:, None] * _w[None, :], 0.0, 1.0)
        _a = jax.random.uniform(jax.random.fold_in(_gk, 2), (8, 2048, 2048)) < _pij
        _a = jnp.logical_or(_a, jnp.eye(2048, dtype=bool))
        _af = _a.astype(jnp.float32)
        _af = _af * jax.random.uniform(jax.random.fold_in(_gk, 3), (8, 2048, 2048), jnp.float32, 0.05, 1)
        adj = _af
        return (x, adj)
    x, adj = _rec_inputs()

    def _L0_gnn_setup():
        import jax, jax.numpy as jnp
        import numpy as np
        ALPHA = 0.2
        key = jax.random.key(seed)
        ks = jax.random.split(key, 6)
        B, N, F_IN, F_OUT = (4, 2048, 128, 128)
        return {'input': jax.random.normal(ks[0], (B, N, F_IN), dtype=jnp.float32), 'adj': jax.random.uniform(ks[1], (B, N, N), dtype=jnp.float32), 'W': jax.random.normal(ks[2], (F_IN, F_OUT), dtype=jnp.float32) * (np.sqrt(2.0) / np.sqrt(F_IN)), 'a1': jax.random.normal(ks[3], (F_OUT, 1), dtype=jnp.float32) * 0.1, 'a2': jax.random.normal(ks[4], (F_OUT, 1), dtype=jnp.float32) * 0.1, 'bias': jax.random.normal(ks[5], (N, F_OUT), dtype=jnp.float32) * 0.02}
    _L0_gnn_all = _L0_gnn_setup()
    _L0_gnn_in = {k: v for k, v in _L0_gnn_all.items() if k in ('W', 'a1', 'a2', 'bias')}
    del _L0_gnn_all
    return {'x': x, 'adj': adj, 'L0_gnn_W': _L0_gnn_in['W'], 'L0_gnn_a1': _L0_gnn_in['a1'], 'L0_gnn_a2': _L0_gnn_in['a2'], 'L0_gnn_bias': _L0_gnn_in['bias']}

def reference(x, adj, L0_gnn_W, L0_gnn_a1, L0_gnn_a2, L0_gnn_bias):
    import jax
    import jax.numpy as jnp

    def _L0_gnn_ref(input, adj, W, a1, a2, bias):
        import jax, jax.numpy as jnp
        import numpy as np
        ALPHA = 0.2
        h = jnp.einsum('bnf,fo->bno', input, W)
        f1 = h @ a1
        f2 = h @ a2
        e = f1 + jnp.swapaxes(f2, 1, 2)
        e = jnp.where(e >= 0, e, ALPHA * e)
        attention = jax.nn.softmax(adj * e, axis=1)
        h_prime = jnp.einsum('bij,bjo->bio', attention, h) + bias[None, :, :]
        return h_prime + input
    x = _L0_gnn_ref(x, adj, L0_gnn_W, L0_gnn_a1, L0_gnn_a2, L0_gnn_bias)
    return x

_drawn_inputs = setup_inputs


def setup_inputs(seed=0):
    import zlib

    import numpy as np

    out = dict(_drawn_inputs(seed))
    spreads = {}
    factors = {'L0_gnn_a1': 3.197, 'L0_gnn_a2': 2.793, 'L0_gnn_bias': 2.837}
    for name, (base, spread) in spreads.items():
        noise = np.random.default_rng([zlib.crc32(name.encode()), seed]).standard_normal(out[name].shape)
        drawn = base * np.exp(spread * noise) if base else spread * noise
        out[name] = jnp.asarray(drawn.astype(out[name].dtype))
    for name, factor in factors.items():
        out[name] = (out[name] * factor).astype(out[name].dtype)
    return out
```

```python
from contextlib import ExitStack

import concourse.bass as bass
from concourse import mybir

ALU = mybir.AluOpType
ACT = mybir.ActivationFunctionType
AX_X = mybir.AxisListType.X
F32 = mybir.dt.float32

P = 128
CHUNK = 512
SLOPE = 0.2
NEG_BIG = -3.4028234663852886e38

AT_BANKS = 3
BLOCK_BUFS = 4
UNIT_COLS = 256
UNIT_BUFS = 4


def gat_kernel(
    nc: bass.Bass,
    x: bass.AP,
    adj: bass.AP,
    W: bass.AP,
    a1: bass.AP,
    a2: bass.AP,
    bias: bass.AP,
    out: bass.AP,
):
    B, N, F = x.shape
    O = W.shape[1]
    assert F == P and O == P and N % CHUNK == 0
    BLOCKS = N // P
    CHUNKS = N // CHUNK
    PER_CHUNK = CHUNK // P
    AT_PER_BATCH = BLOCKS * CHUNKS
    HCOLS = O + 2
    H_PER_BANK = CHUNK // HCOLS
    UNITS = N // UNIT_COLS
    PER_UNIT = UNIT_COLS // P
    assert UNITS % UNIT_BUFS == 0 and BLOCKS % BLOCK_BUFS == 0

    at_bank = [i % AT_BANKS for i in range(AT_PER_BATCH)]

    def chunk_before(i):
        j = i - 1
        while at_bank[j % AT_PER_BATCH] != at_bank[i]:
            j -= 1
        return j

    h_parts = [list(range(a, min(a + H_PER_BANK, BLOCKS))) for a in range(0, BLOCKS, H_PER_BANK)]
    NH = len(h_parts)
    O_PIECES = [(1 + q // 2, q % 2, "O", q) for q in range(CHUNKS)]
    X_PIECES = [(3 + q // 2, q % 2, "X", q) for q in range(CHUNKS)]
    H_PIECES = [(5 + q // 2, q % 2, "H", q) for q in range(NH)]
    F_PIECES = [(9 + q // 2, q % 2, "F", q) for q in range(CHUNKS)]
    NEXT_PIECES = X_PIECES + H_PIECES + F_PIECES
    PER_BODY = len(O_PIECES) + len(NEXT_PIECES)

    def pieces(first, last):
        found = ([] if first else O_PIECES) + ([] if last else NEXT_PIECES)
        return sorted(found)

    def side_base(b):
        if isinstance(b, int) and b == 0:
            return len(NEXT_PIECES)
        if isinstance(b, int) and b == B:
            return PER_BODY * b - len(O_PIECES)
        return PER_BODY * b + len(NEXT_PIECES) - len(O_PIECES)

    HALVES = [slice(0, BLOCKS // 2), slice(BLOCKS // 2, BLOCKS)]

    adj_units = adj.rearrange("b (t p) (u c) -> b u p t c", p=P, c=UNIT_COLS)
    x_rows = x.rearrange("b (t p) f -> b p t f", p=P)
    out_rows = out.rearrange("b (t p) f -> b p t f", p=P)
    bias_rows = bias.rearrange("(t p) f -> p t f", p=P)

    with ExitStack() as ctx:
        def sb(name, shape):
            return ctx.enter_context(nc.sbuf_tensor(name, shape, F32))

        def psum(name, shape):
            return ctx.enter_context(nc.psum_tensor(name, shape, F32))

        def sem(name):
            return ctx.enter_context(nc.semaphore(name))

        adj_sb = sb("adj_sb", [P, UNIT_BUFS, BLOCKS, UNIT_COLS])
        block = sb("block", [P, BLOCK_BUFS, N])
        f1_all = sb("f1_all", [P, 2, N])
        h_all = sb("h_all", [P, 2, BLOCKS, HCOLS])
        f1_col = sb("f1_col", [P, BLOCKS])
        x_in = sb("x_in", [P, BLOCKS, F])
        xT = sb("xT", [P, N])
        x_bias = sb("x_bias", [P, 2, BLOCKS, F])
        bias_sb = sb("bias_sb", [P, BLOCKS, F])
        outT_sb = sb("outT_sb", [P, N])
        out_sb = sb("out_sb", [P, BLOCKS, O])
        hn = sb("hn", [P, 2, O])
        chunk_max = sb("chunk_max", [P, 2, CHUNKS])
        neg_max = sb("neg_max", [P, 2, 1])
        z_sum = sb("z_sum", [P, 2, 1])
        z_inv = sb("z_inv", [P, 2, 1])
        ident = sb("ident", [P, P])
        w_ext = sb("w_ext", [P, HCOLS])
        wT = sb("wT", [P, P])
        a12 = sb("a12", [P, 2])

        outT_ps = psum("outT_ps", [P, CHUNKS, CHUNK])
        at_ps = psum("at_ps", [P, AT_BANKS, CHUNK])
        side_ps = psum("side_ps", [P, CHUNK])

        weights_landed = sem("weights_landed")
        bias_landed = sem("bias_landed")
        x_landed = sem("x_landed")
        x_added = sem("x_added")
        adj_landed = [sem(f"adj_landed{i}") for i in range(UNIT_BUFS)]
        zeroed = sem("zeroed")
        ident_ready = sem("ident_ready")
        wT_made = sem("wT_made")
        wT_copied = sem("wT_copied")
        wa_made = sem("wa_made")
        w_ext_ready = sem("w_ext_ready")
        adj_transposed = sem("adj_transposed")
        t_done = sem("t_done")
        e_done = sem("e_done")
        s_done = sem("s_done")
        max_done = sem("max_done")
        exp_done = sem("exp_done")
        inv_done = sem("inv_done")
        hn_done = sem("hn_done")
        mm_done = sem("mm_done")
        outT_copied = sem("outT_copied")
        side_made = sem("side_made")
        side_drained = sem("side_drained")
        f1_copied = sem("f1_copied")
        out_stored = sem("out_stored")

        code = ctx.enter_context(nc.Block())

        def batches(eng, body):
            body(0, True, False)
            with eng.Fori(1, B - 1) as b:
                body(b, False, False)
            body(B - 1, False, True)

        def wait(eng, s, value):
            if not isinstance(value, int) or value > 0:
                eng.wait_ge(s, value)

        def parity(b):
            return b % 2

        @code.sync
        def _(sp):
            sp.dma_start(w_ext[:, 0:O], W).then_inc(weights_landed, 16)
            sp.dma_start(a12[:, 0:1], a1).then_inc(weights_landed, 16)
            sp.dma_start(a12[:, 1:2], a2).then_inc(weights_landed, 16)
            for half in HALVES:
                sp.dma_start(x_in[:, half], x_rows[0, :, half]).then_inc(x_landed, 16)

            def load_adj(b, m, wait_for):
                if wait_for is not None:
                    sp.wait_ge(adj_transposed, wait_for)
                sp.dma_start(adj_sb[:, m % UNIT_BUFS], adj_units[b, m]).then_inc(
                    adj_landed[m % UNIT_BUFS], 16)

            def load_x(b, x_pieces):
                sp.wait_ge(side_made, x_pieces)
                sp.wait_ge(x_added, CHUNKS * b)
                for half in HALVES:
                    sp.dma_start(x_in[:, half], x_rows[b, :, half]).then_inc(x_landed, 16)

            def store_out(b):
                sp.wait_ge(side_drained, side_base(b + 1) + len(O_PIECES))
                sp.dma_start(out_rows[b], out_sb[:]).then_inc(out_stored, 16)

            per_unit = PER_UNIT * CHUNKS

            def load_batch(b, first, last):
                for m in range(UNITS):
                    count = b * UNITS + m - UNIT_BUFS + 1
                    if not first and m == 6:
                        store_out(b - 1)
                    load_adj(b, m, None if first and m < UNIT_BUFS else count * per_unit)
                    if first and m == 1:
                        for half in HALVES:
                            sp.dma_start(bias_sb[:, half], bias_rows[:, half]).then_inc(bias_landed, 16)
                    if first and m == 2:
                        load_x(1, len(X_PIECES))
                    if not first and not last and m == 0:
                        load_x(b + 1, side_base(b) - len(NEXT_PIECES) + len(X_PIECES))

            batches(sp, load_batch)
            store_out(B - 1)
            sp.wait_ge(out_stored, 16 * B)

        @code.gpsimd
        def _(pool):
            pool.memset(ident[:], 0.0).then_inc(zeroed, 1)
            pool.wait_ge(zeroed, 1)
            pool.affine_select(out=ident[:], in_=ident[:], compare_op=ALU.not_equal, fill=1.0, base=0,
                               pattern=[[-1, P]], channel_multiplier=1).then_inc(ident_ready, 1)

            def add_bias(b, q):
                rows = slice(q * PER_CHUNK, (q + 1) * PER_CHUNK)
                pool.tensor_tensor(x_bias[:, parity(b), rows, :], x_in[:, rows, :], bias_sb[:, rows, :],
                                   ALU.add).then_inc(x_added, 1)

            def copy_f1(b, side_count):
                pool.wait_ge(side_drained, side_count)
                pool.tensor_copy(f1_col[:], h_all[:, parity(b), :, O]).then_inc(f1_copied, 1)

            pool.wait_ge(bias_landed, 32)
            pool.wait_ge(x_landed, 32)
            for q in range(CHUNKS):
                add_bias(0, q)
            copy_f1(0, len(X_PIECES) + NH)

            def body(b, first, last):
                for n in range(BLOCKS):
                    k = BLOCKS * b + n
                    if not last and n == 8:
                        copy_f1(b + 1, side_base(b) + sum(1 for p in pieces(first, last) if p[2] in "OXH"))
                    pool.wait_ge(inv_done, k + 1)
                    wait(pool, mm_done, CHUNKS * (k - 1))
                    pool.tensor_tensor(hn[:, n % 2, :], h_all[:, parity(b), n, 0:O],
                                       z_inv[:, n % 2, :].broadcast_to([P, O]), ALU.mult).then_inc(hn_done, 1)
                    if not last and n in (3, 4, 5, 6):
                        if n == 3:
                            pool.wait_ge(x_landed, 32 * (b + 2))
                            if not first:
                                pool.wait_ge(side_drained, side_base(b) + len(O_PIECES))
                        add_bias(b + 1, n - 3)

            batches(pool, body)

        @code.scalar
        def _(act):
            def drain(b, kind, part, count):
                act.wait_ge(side_made, count)
                if kind == "X":
                    act.copy(xT[:, part * CHUNK:(part + 1) * CHUNK], side_ps[:]).then_inc(side_drained, 1)
                elif kind == "H":
                    rows = h_parts[part]
                    act.copy(h_all[:, parity(b), rows[0]:rows[-1] + 1, :],
                             side_ps[:, 0:len(rows) * HCOLS].rearrange("p (r c) -> p r c", c=HCOLS)
                             ).then_inc(side_drained, 1)
                elif kind == "F":
                    act.copy(f1_all[:, parity(b), part * CHUNK:(part + 1) * CHUNK],
                             side_ps[:]).then_inc(side_drained, 1)

            def add_f(b, n, count):
                wait(act, mm_done, CHUNKS * (count - BLOCK_BUFS + 1))
                act.activation(block[:, n % BLOCK_BUFS, :], f1_all[:, parity(b), :], ACT.Identity,
                               bias=h_all[:, parity(b), n, O + 1:O + 2], scale=1.0).then_inc(t_done, 1)

            act.wait_ge(wT_made, 1)
            act.copy(wT[:], side_ps[:, 0:P]).then_inc(wT_copied, 1)
            act.wait_ge(wa_made, 1)
            act.copy(w_ext[:, O:HCOLS], side_ps[:, 0:2]).then_inc(w_ext_ready, 1)
            for i, (_, _, kind, part) in enumerate(NEXT_PIECES):
                drain(0, kind, part, i + 1)
            act.wait_ge(side_drained, len(NEXT_PIECES))
            add_f(0, 0, 0)
            add_f(0, 1, 1)

            def body(b, first, last):
                todo = [(step, place, kind, part, i) for i, (step, place, kind, part)
                        in enumerate(pieces(first, last))]

                def side(step, place):
                    for s, p, kind, part, i in todo:
                        if (s, p) == (step, place) and kind != "O":
                            drain(b + 1, kind, part, side_base(b) + i + 1)

                for n in range(BLOCKS):
                    k = BLOCKS * b + n
                    side(n - 1, 1)
                    if n + 2 < BLOCKS:
                        add_f(b, n + 2, k + 2)
                    elif not last:
                        if n + 2 == BLOCKS:
                            act.wait_ge(side_drained, side_base(b) + len(todo))
                        add_f(b + 1, n + 2 - BLOCKS, k + 2)
                    act.wait_ge(max_done, k + 1)
                    wait(act, inv_done, k - 1)
                    E = block[:, n % BLOCK_BUFS, :]
                    act.activation(E, E, ACT.Exp, bias=neg_max[:, n % 2, :], scale=1.0,
                                   accum_out=z_sum[:, n % 2, :]).then_inc(exp_done, 1)
                    side(n, 0)
                    if n == 0 and not first:
                        copy_outT(b - 1)

            def copy_outT(b):
                for c in range(CHUNKS // 2):
                    act.wait_ge(mm_done, CHUNKS * (BLOCKS * b + BLOCKS - 1) + c + 1)
                    act.copy(outT_sb[:, c * CHUNK:(c + 1) * CHUNK], outT_ps[:, c, :]).then_inc(outT_copied, 1)

            batches(act, body)
            copy_outT(B - 1)

        @code.vector
        def _(dve):
            def leaky(n, count):
                dve.wait_ge(t_done, count + 1)
                t = block[:, n % BLOCK_BUFS, :]
                dve.scalar_tensor_tensor(out=t, in0=t, scalar=SLOPE, in1=t, op0=ALU.mult,
                                         op1=ALU.max).then_inc(e_done, 1)

            def add_residual(b, part, count):
                dve.wait_ge(side_made, count)
                wait(dve, out_stored, 16 * b)
                dve.wait_ge(x_added, CHUNKS * (b + 1))
                rows = slice(part * PER_CHUNK, (part + 1) * PER_CHUNK)
                dve.tensor_tensor(out_sb[:, rows, :], side_ps[:].rearrange("p (r o) -> p r o", o=O),
                                  x_bias[:, parity(b), rows, :], ALU.add).then_inc(side_drained, 1)

            def copy_outT(b):
                for c in range(CHUNKS // 2, CHUNKS):
                    dve.wait_ge(mm_done, CHUNKS * (BLOCKS * b + BLOCKS - 1) + c + 1)
                    dve.tensor_copy(outT_sb[:, c * CHUNK:(c + 1) * CHUNK], outT_ps[:, c, :]).then_inc(outT_copied, 1)

            def invert(n, count):
                dve.wait_ge(exp_done, count + 1)
                wait(dve, hn_done, count - 1)
                dve.reciprocal(z_inv[:, n % 2, :], z_sum[:, n % 2, :]).then_inc(inv_done, 1)

            counts = [dve.alloc_register(f"chunk_count{i}") for i in range(2)]
            dve.reg_mov(counts[0], AT_PER_BATCH + 1)

            leaky(0, 0)

            def body(b, first, last):
                todo = [(step, place, kind, part, i) for i, (step, place, kind, part)
                        in enumerate(pieces(first, last))]

                def side(step, place):
                    for s, p, kind, part, i in todo:
                        if (s, p) == (step, place) and kind == "O":
                            add_residual(b - 1, part, side_base(b) + i + 1)

                static = first or last
                for n in range(BLOCKS):
                    k = BLOCKS * b + n
                    dve.wait_ge(e_done, k + 1)
                    for c in range(CHUNKS):
                        at = n * CHUNKS + c
                        if static:
                            dve.wait_ge(adj_transposed, CHUNKS * k + c + 1)
                        else:
                            dve.wait_ge(adj_transposed, counts[at % 2])
                            dve.reg_add(counts[(at + 1) % 2], counts[at % 2], 1)
                        chunk = block[:, n % BLOCK_BUFS, c * CHUNK:(c + 1) * CHUNK]
                        dve.tensor_tensor_reduce(chunk, at_ps[:, at_bank[at], :], chunk, 1.0, NEG_BIG,
                                                 ALU.mult, ALU.max, chunk_max[:, n % 2, c:c + 1]
                                                 ).then_inc(s_done, 1)
                        if c == 0 and not (first and n == 0):
                            invert((n - 1) % BLOCKS, k - 1)
                    side(n - 1, 1)
                    dve.wait_ge(s_done, CHUNKS * (k + 1))
                    wait(dve, exp_done, k - 1)
                    dve.tensor_reduce(neg_max[:, n % 2, :], chunk_max[:, n % 2, :], AX_X, ALU.max,
                                      negate=True).then_inc(max_done, 1)
                    if not (last and n == BLOCKS - 1):
                        leaky((n + 1) % BLOCKS, k + 1)
                    if n == 0 and not first:
                        copy_outT(b - 1)
                    side(n, 0)

            batches(dve, body)
            invert(BLOCKS - 1, B * BLOCKS - 1)
            copy_outT(B - 1)
            for q in range(CHUNKS):
                add_residual(B - 1, q, side_base(B) + q + 1)

        @code.tensor
        def _(pe):
            def transpose_chunk(b, n, c):
                m, half = n // PER_UNIT, n % PER_UNIT
                at = n * CHUNKS + c
                if c == 0 and half == 0:
                    pe.wait_ge(adj_landed[m % UNIT_BUFS], 16 * (UNITS // UNIT_BUFS * b + m // UNIT_BUFS + 1))
                wait(pe, s_done, AT_PER_BATCH * b + chunk_before(at) + 1)
                for r in range(PER_CHUNK):
                    last = pe.transpose(at_ps[:, at_bank[at], r * P:(r + 1) * P],
                                        adj_sb[:, m % UNIT_BUFS, c * PER_CHUNK + r, half * P:(half + 1) * P],
                                        ident[:])
                last.then_inc(adj_transposed, 1)

            def multiply_chunk(b, n, c):
                count = BLOCKS * b + n
                if c == 0:
                    pe.wait_ge(hn_done, count + 1)
                if n == 0:
                    wait(pe, outT_copied, CHUNKS * b)
                pe.matmul(outT_ps[:, c, :], hn[:, n % 2, :], block[:, n % BLOCK_BUFS, c * CHUNK:(c + 1) * CHUNK],
                          start=(n == 0), stop=(n == BLOCKS - 1)).then_inc(mm_done, 1)

            def side_piece(b, kind, part, count):
                wait(pe, side_drained, count - 1)
                if kind == "X":
                    if part == 0:
                        pe.wait_ge(x_landed, 32 * (b + 1))
                    for r in range(PER_CHUNK):
                        last = pe.transpose(side_ps[:, r * P:(r + 1) * P], x_in[:, part * PER_CHUNK + r, :], ident[:])
                    last.then_inc(side_made, 1)
                elif kind == "H":
                    for i, r in enumerate(h_parts[part]):
                        last = pe.matmul(side_ps[:, i * HCOLS:(i + 1) * HCOLS], xT[:, r * P:(r + 1) * P], w_ext[:],
                                         start=True, stop=True)
                    last.then_inc(side_made, 1)
                elif kind == "F":
                    if part == 0:
                        pe.wait_ge(f1_copied, b + 1)
                    for r in range(PER_CHUNK):
                        col = part * PER_CHUNK + r
                        last = pe.transpose(side_ps[:, r * P:(r + 1) * P],
                                            f1_col[:, col:col + 1].broadcast_to([P, P]), ident[:])
                    last.then_inc(side_made, 1)
                else:
                    if part == 0:
                        pe.wait_ge(outT_copied, CHUNKS * (b + 1))
                    for r in range(PER_CHUNK):
                        last = pe.transpose(side_ps[:, r * P:(r + 1) * P],
                                            outT_sb[:, (part * PER_CHUNK + r) * P:(part * PER_CHUNK + r + 1) * P],
                                            ident[:])
                    last.then_inc(side_made, 1)

            pe.wait_ge(ident_ready, 1)
            pe.wait_ge(weights_landed, 48)
            pe.transpose(side_ps[:, 0:P], w_ext[:, 0:O], ident[:]).then_inc(wT_made, 1)
            pe.wait_ge(wT_copied, 1)
            pe.matmul(side_ps[:, 0:2], wT[:], a12[:], start=True, stop=True).then_inc(wa_made, 1)
            pe.wait_ge(w_ext_ready, 1)
            for i, (_, _, kind, part) in enumerate(NEXT_PIECES):
                side_piece(0, kind, part, i + 1)
            for c in range(AT_BANKS):
                transpose_chunk(0, 0, c)

            def body(b, first, last):
                todo = [(step, place, kind, part, i) for i, (step, place, kind, part)
                        in enumerate(pieces(first, last))]

                def side(step, place):
                    for s, p, kind, part, i in todo:
                        if (s, p) == (step, place):
                            side_piece(b - 1 if kind == "O" else b + 1, kind, part, side_base(b) + i + 1)

                for n in range(BLOCKS):
                    transpose_chunk(b, n, CHUNKS - 1)
                    for c in range(CHUNKS):
                        if n > 0:
                            multiply_chunk(b, n - 1, c)
                        elif not first:
                            multiply_chunk(b - 1, BLOCKS - 1, c)
                        if c < CHUNKS - 1:
                            if n + 1 < BLOCKS:
                                transpose_chunk(b, n + 1, c)
                            elif not last:
                                transpose_chunk(b + 1, 0, c)
                        if c == 1:
                            side(n, 0)
                    side(n, 1)

            batches(pe, body)
            for c in range(CHUNKS):
                multiply_chunk(B - 1, BLOCKS - 1, c)
            for q in range(CHUNKS):
                side_piece(B - 1, "O", q, side_base(B) + q + 1)


_INS = ["x", "adj", "L0_gnn_W", "L0_gnn_a1", "L0_gnn_a2", "L0_gnn_bias"]


def kernel(**inputs):
    import numpy as _np
    import concourse.bacc as _bacc
    from concourse import mybir as _mybir
    from concourse.bass_utils import run_bass_kernel_spmd as _run

    nc = _bacc.Bacc("TRN2", target_bir_lowering=False, num_devices=1)
    arrays, args = {}, []
    for name in _INS:
        a = _np.ascontiguousarray(inputs[name])
        arrays[f"in_{name}_dram"] = a
        args.append(nc.dram_tensor(f"in_{name}_dram", a.shape, _mybir.dt.from_np(a.dtype), kind="ExternalInput").ap())
    args.append(nc.dram_tensor("out_0_dram", tuple(inputs["x"].shape), F32, kind="ExternalOutput").ap())
    gat_kernel(nc, *args)
    r = _run(nc, [arrays], core_ids=[0])
    return r.results[0]["out_0_dram"]
```

```python
from contextlib import ExitStack

import concourse.bass as bass
from concourse import mybir

ALU = mybir.AluOpType
ACT = mybir.ActivationFunctionType
AX_X = mybir.AxisListType.X
F32 = mybir.dt.float32

P = 128
CHUNK = 512
SLOPE = 0.2
NEG_BIG = -3.4028234663852886e38

AT_BANKS = 3
BLOCK_BUFS = 4
UNIT_COLS = 256
UNIT_BUFS = 4


def gat_kernel(
    nc: bass.Bass,
    x: bass.AP,
    adj: bass.AP,
    W: bass.AP,
    a1: bass.AP,
    a2: bass.AP,
    bias: bass.AP,
    out: bass.AP,
):
    B, N, F = x.shape
    O = W.shape[1]
    assert F == P and O == P and N % CHUNK == 0
    BLOCKS = N // P
    CHUNKS = N // CHUNK
    PER_CHUNK = CHUNK // P
    AT_PER_BATCH = BLOCKS * CHUNKS
    UNITS = N // UNIT_COLS
    PER_UNIT = UNIT_COLS // P
    assert UNITS % UNIT_BUFS == 0 and BLOCKS % BLOCK_BUFS == 0

    at_bank = [i % AT_BANKS for i in range(AT_PER_BATCH)]

    def chunk_before(i):
        j = i - 1
        while at_bank[j % AT_PER_BATCH] != at_bank[i]:
            j -= 1
        return j

    O_PIECES = [(1 + q // 2, q % 2, "O", q) for q in range(CHUNKS)]
    F_PIECES = [(10, 1, "F", 0)]
    FIRST_ADD = BLOCKS - 1 - CHUNKS
    PER_BODY = len(O_PIECES) + len(F_PIECES)
    DOTS = [(kind, q) for q in range(CHUNKS) for kind in range(2)]
    assert len(DOTS) + 2 <= F_PIECES[0][0] and F_PIECES[-1][0] + 2 < BLOCKS

    def pieces(first, last):
        found = ([] if first else O_PIECES) + ([] if last else F_PIECES)
        return sorted(found)

    def side_base(b):
        if isinstance(b, int) and b == 0:
            return 0
        if isinstance(b, int) and b == B:
            return PER_BODY * (b - 1)
        return PER_BODY * b - len(O_PIECES)

    HALVES = [slice(0, BLOCKS // 2), slice(BLOCKS // 2, BLOCKS)]

    def dots_before(b):
        return BLOCKS + 2 * BLOCKS * b

    adj_units = adj.rearrange("b (t p) (u c) -> b u p t c", p=P, c=UNIT_COLS)
    x_rows = x.rearrange("b (t p) f -> b p t f", p=P)
    out_rows = out.rearrange("b (t p) f -> b p t f", p=P)
    bias_rows = bias.rearrange("(t p) f -> p t f", p=P)

    f1_dram = nc.dram_tensor("f1_dram", [BLOCKS, P], F32).ap()

    with ExitStack() as ctx:
        def sb(name, shape):
            return ctx.enter_context(nc.sbuf_tensor(name, shape, F32))

        def psum(name, shape):
            return ctx.enter_context(nc.psum_tensor(name, shape, F32))

        def sem(name):
            return ctx.enter_context(nc.semaphore(name))

        adj_sb = sb("adj_sb", [P, UNIT_BUFS, BLOCKS, UNIT_COLS])
        block = sb("block", [P, BLOCK_BUFS, N])
        f1_all = sb("f1_all", [P, 2, N])
        f1_rows = sb("f1_rows", [BLOCKS, P])
        f_new = sb("f_new", [P, 2, BLOCKS])
        f2_all = sb("f2_all", [P, 2, BLOCKS])
        x_in = sb("x_in", [P, 2, BLOCKS, F])
        products = sb("products", [P, 2, BLOCKS, F])
        bias_sb = sb("bias_sb", [P, BLOCKS, F])
        yT_sb = sb("yT_sb", [P, N])
        out_sb = sb("out_sb", [P, BLOCKS, O])
        xn = sb("xn", [P, 2, F])
        chunk_max = sb("chunk_max", [P, 2, CHUNKS])
        neg_max = sb("neg_max", [P, 2, 1])
        z_sum = sb("z_sum", [P, 2, 1])
        z_inv = sb("z_inv", [P, 2, 1])
        ident = sb("ident", [P, P])
        w_sb = sb("w_sb", [P, O])
        wa_rows = sb("wa_rows", [P, 2, F])
        wT = sb("wT", [P, P])
        a12 = sb("a12", [P, 2])

        yT_ps = psum("yT_ps", [P, CHUNKS, CHUNK])
        at_ps = psum("at_ps", [P, AT_BANKS, CHUNK])
        side_ps = psum("side_ps", [P, CHUNK])

        weights_landed = sem("weights_landed")
        bias_landed = sem("bias_landed")
        x_landed = sem("x_landed")
        x_added = sem("x_added")
        multiplied = sem("multiplied")
        dots_done = sem("dots_done")
        first_f1 = sem("first_f1")
        f1_stored = sem("f1_stored")
        f1_spread = sem("f1_spread")
        f2_copied = sem("f2_copied")
        adj_landed = [sem(f"adj_landed{i}") for i in range(UNIT_BUFS)]
        zeroed = sem("zeroed")
        ident_ready = sem("ident_ready")
        wT_made = sem("wT_made")
        wT_copied = sem("wT_copied")
        wa_made = sem("wa_made")
        wa_ready = sem("wa_ready")
        adj_transposed = sem("adj_transposed")
        t_done = sem("t_done")
        e_done = sem("e_done")
        s_done = sem("s_done")
        max_done = sem("max_done")
        exp_done = sem("exp_done")
        inv_done = sem("inv_done")
        xn_done = sem("xn_done")
        mm_done = sem("mm_done")
        yT_copied = sem("yT_copied")
        first_made = sem("first_made")
        first_drained = [sem("first_drained_act"), sem("first_drained_dve")]
        side_made = sem("side_made")
        side_drained = sem("side_drained")
        out_stored = sem("out_stored")

        code = ctx.enter_context(nc.Block())

        def batches(eng, body):
            body(0, True, False)
            with eng.Fori(1, B - 1) as b:
                body(b, False, False)
            body(B - 1, False, True)

        def wait(eng, s, value):
            if not isinstance(value, int) or value > 0:
                eng.wait_ge(s, value)

        def parity(b):
            return b % 2

        def first_piece(q):
            return f1_all[:, 0, q * CHUNK:(q + 1) * CHUNK], yT_ps[:, q, :]

        def quarter(q):
            return slice(q * PER_CHUNK, (q + 1) * PER_CHUNK)

        @code.sync
        def _(sp):
            sp.dma_start(w_sb[:], W).then_inc(weights_landed, 16)
            sp.dma_start(a12[:, 0:1], a1).then_inc(weights_landed, 16)
            sp.dma_start(a12[:, 1:2], a2).then_inc(weights_landed, 16)
            for half in HALVES:
                sp.dma_start(x_in[:, 0, half], x_rows[0, :, half]).then_inc(x_landed, 16)

            def load_adj(b, m, wait_for):
                if wait_for is not None:
                    sp.wait_ge(adj_transposed, wait_for)
                sp.dma_start(adj_sb[:, m % UNIT_BUFS], adj_units[b, m]).then_inc(
                    adj_landed[m % UNIT_BUFS], 16)

            def load_x(b, first):
                if first:
                    sp.wait_ge(first_f1, 1)
                    sp.wait_ge(multiplied, 1)
                else:
                    sp.wait_ge(xn_done, BLOCKS * (b - 1))
                for half in HALVES:
                    sp.dma_start(x_in[:, parity(b), half], x_rows[b, :, half]).then_inc(x_landed, 16)

            def store_out(b):
                sp.wait_ge(side_drained, side_base(b + 1) + len(O_PIECES))
                sp.dma_start(out_rows[b], out_sb[:]).then_inc(out_stored, 16)

            def spread_f1(b):
                sp.wait_ge(side_drained, side_base(b))
                sp.dma_start(f1_dram, f1_rows[:]).then_inc(f1_stored, 16)
                sp.wait_ge(f1_stored, 16 * b)
                sp.dma_start(f1_all[:, parity(b), :].rearrange("p (o i) -> p o i", o=1),
                             f1_dram.rearrange("(o t) p -> o (t p)", o=1).partition_broadcast(P)).then_inc(f1_spread, 16)

            per_unit = PER_UNIT * CHUNKS

            def load_batch(b, first, last):
                for m in range(UNITS):
                    count = b * UNITS + m - UNIT_BUFS + 1
                    if not first and m == 6:
                        store_out(b - 1)
                    if not first and m == 1:
                        spread_f1(b)
                    load_adj(b, m, None if first and m < UNIT_BUFS else count * per_unit)
                    if first and m == 1:
                        for half in HALVES:
                            sp.dma_start(bias_sb[:, half], bias_rows[:, half]).then_inc(bias_landed, 16)
                    if not last and m == 2:
                        load_x(b + 1, first)

            batches(sp, load_batch)
            for q in range(CHUNKS):
                sp.wait_ge(side_drained, side_base(B) + q + 1)
                rows = slice(q * PER_CHUNK, (q + 1) * PER_CHUNK)
                sp.dma_start(out_rows[B - 1, :, rows], out_sb[:, rows]).then_inc(out_stored, 16)
            sp.wait_ge(out_stored, 16 * (B - 1 + CHUNKS))

        @code.gpsimd
        def _(pool):
            pool.memset(ident[:], 0.0).then_inc(zeroed, 1)
            pool.wait_ge(zeroed, 1)
            pool.affine_select(out=ident[:], in_=ident[:], compare_op=ALU.not_equal, fill=1.0, base=0,
                               pattern=[[-1, P]], channel_multiplier=1).then_inc(ident_ready, 1)

            def multiply(b, kind, q):
                if (kind, q) == DOTS[0]:
                    pool.wait_ge(x_landed, 32 * (b + 1))
                wa = wa_rows[:, kind:kind + 1, :].broadcast_to([P, PER_CHUNK, F])
                pool.tensor_tensor(products[:, kind, quarter(q), :], x_in[:, parity(b), quarter(q), :], wa,
                                   ALU.mult).then_inc(multiplied, 1)

            def copy_f2(b, dots):
                pool.wait_ge(dots_done, dots)
                pool.tensor_copy(f2_all[:, parity(b), :], f_new[:, 1, :]).then_inc(f2_copied, 1)

            def add_bias(b, q):
                pool.tensor_tensor(out_sb[:, quarter(q), :], x_in[:, parity(b), quarter(q), :],
                                   bias_sb[:, quarter(q), :], ALU.add).then_inc(x_added, 1)

            pool.wait_ge(wa_ready, 2)
            pool.wait_ge(x_landed, 32)
            for q in range(CHUNKS):
                multiply(0, 1, q)
            copy_f2(0, dots_before(0))
            pool.wait_ge(bias_landed, 32)

            def body(b, first, last):
                for n in range(BLOCKS):
                    k = BLOCKS * b + n
                    if n == FIRST_ADD:
                        wait(pool, out_stored, 16 * b)
                    pool.wait_ge(inv_done, k + 1)
                    wait(pool, mm_done, CHUNKS * (k - 1))
                    pool.tensor_tensor(xn[:, n % 2, :], x_in[:, parity(b), n, :],
                                       z_inv[:, n % 2, :].broadcast_to([P, F]), ALU.mult).then_inc(xn_done, 1)
                    if not last:
                        if 1 <= n <= len(DOTS):
                            multiply(b + 1, *DOTS[n - 1])
                        elif n == len(DOTS) + 2:
                            copy_f2(b + 1, dots_before(b + 1))
                    if FIRST_ADD <= n < FIRST_ADD + CHUNKS:
                        add_bias(b, n - FIRST_ADD)

            batches(pool, body)

        @code.scalar
        def _(act):
            def take_f1(count):
                act.wait_ge(side_made, count)
                act.copy(f1_rows[:], side_ps[0:BLOCKS, 0:P]).then_inc(side_drained, 1)

            def sum_dots(kind, q, count):
                act.wait_ge(multiplied, count)
                for r in range(q * PER_CHUNK, (q + 1) * PER_CHUNK):
                    product = products[:, kind, r, :]
                    act.activation(product, product, ACT.Identity, bias=0.0, scale=1.0,
                                   accum_out=f_new[:, kind, r:r + 1]).then_inc(dots_done, 1)

            def add_f(b, n, count):
                wait(act, mm_done, CHUNKS * (count - BLOCK_BUFS + 1))
                act.activation(block[:, n % BLOCK_BUFS, :], f1_all[:, parity(b), :], ACT.Identity,
                               bias=f2_all[:, parity(b), n:n + 1], scale=1.0).then_inc(t_done, 1)

            act.wait_ge(wT_made, 1)
            act.copy(wT[:], side_ps[:, 0:P]).then_inc(wT_copied, 1)
            for kind in range(2):
                act.wait_ge(wa_made, kind + 1)
                act.copy(wa_rows[:, kind, :], at_ps[:, kind, 0:F]).then_inc(wa_ready, 1)
            for q in range(CHUNKS):
                sum_dots(1, q, q + 1)
            for q in range(0, CHUNKS, 2):
                act.wait_ge(first_made, q + 1)
                act.copy(*first_piece(q)).then_inc(first_drained[0], 1)
            for engine in range(2):
                act.wait_ge(first_drained[engine], CHUNKS // 2)
            act.wait_ge(f2_copied, 1)
            add_f(0, 0, 0)
            add_f(0, 1, 1)

            def body(b, first, last):
                todo = [(step, place, kind, part, i) for i, (step, place, kind, part)
                        in enumerate(pieces(first, last))]

                def side(step, place):
                    for s, p, kind, part, i in todo:
                        if (s, p) == (step, place) and kind == "F":
                            take_f1(side_base(b) + i + 1)

                for n in range(BLOCKS):
                    k = BLOCKS * b + n
                    side(n - 1, 1)
                    if n + 2 < BLOCKS:
                        add_f(b, n + 2, k + 2)
                    elif not last:
                        if n + 2 == BLOCKS:
                            act.wait_ge(f1_spread, 16 * (b + 1))
                            act.wait_ge(f2_copied, b + 2)
                        add_f(b + 1, n + 2 - BLOCKS, k + 2)
                    act.wait_ge(max_done, k + 1)
                    wait(act, inv_done, k - 1)
                    E = block[:, n % BLOCK_BUFS, :]
                    act.activation(E, E, ACT.Exp, bias=neg_max[:, n % 2, :], scale=1.0,
                                   accum_out=z_sum[:, n % 2, :]).then_inc(exp_done, 1)
                    side(n, 0)
                    if not last and 2 <= n < 2 + len(DOTS):
                        sum_dots(*DOTS[n - 2], CHUNKS + len(DOTS) * b + n - 1)
                    if n == 0 and not first:
                        copy_yT(b - 1, CHUNKS)

            def copy_yT(b, chunks):
                for c in range(chunks):
                    act.wait_ge(mm_done, CHUNKS * (BLOCKS * b + BLOCKS - 1) + c + 1)
                    act.copy(yT_sb[:, c * CHUNK:(c + 1) * CHUNK], yT_ps[:, c, :]).then_inc(yT_copied, 1)

            batches(act, body)
            copy_yT(B - 1, CHUNKS // 2)

        @code.vector
        def _(dve):
            def leaky(n, count):
                dve.wait_ge(t_done, count + 1)
                t = block[:, n % BLOCK_BUFS, :]
                dve.scalar_tensor_tensor(out=t, in0=t, scalar=SLOPE, in1=t, op0=ALU.mult,
                                         op1=ALU.max).then_inc(e_done, 1)

            def add_residual(b, part, count):
                dve.wait_ge(side_made, count)
                dve.wait_ge(x_added, CHUNKS * b + part + 1)
                rows = out_sb[:, quarter(part), :]
                dve.tensor_tensor(rows, side_ps[:].rearrange("p (r o) -> p r o", o=O), rows, ALU.add
                                  ).then_inc(side_drained, 1)

            def invert(n, count):
                dve.wait_ge(exp_done, count + 1)
                wait(dve, xn_done, count - 1)
                dve.reciprocal(z_inv[:, n % 2, :], z_sum[:, n % 2, :]).then_inc(inv_done, 1)

            counts = [dve.alloc_register(f"chunk_count{i}") for i in range(2)]
            dve.reg_mov(counts[0], AT_PER_BATCH + 1)

            dve.wait_ge(wa_ready, 1)
            dve.wait_ge(x_landed, 32)
            for r in range(BLOCKS):
                dve.tensor_tensor_reduce(products[:, 0, r, :], x_in[:, 0, r, :], wa_rows[:, 0, :], 1.0, 0.0,
                                         ALU.mult, ALU.add, f_new[:, 0, r:r + 1]).then_inc(first_f1, 1)
            for q in range(1, CHUNKS, 2):
                dve.wait_ge(first_made, q + 1)
                dve.tensor_copy(*first_piece(q)).then_inc(first_drained[1], 1)
            leaky(0, 0)

            def body(b, first, last):
                todo = [(step, place, kind, part, i) for i, (step, place, kind, part)
                        in enumerate(pieces(first, last))]

                def side(step, place):
                    for s, p, kind, part, i in todo:
                        if (s, p) == (step, place) and kind == "O":
                            add_residual(b - 1, part, side_base(b) + i + 1)

                static = first or last
                for n in range(BLOCKS):
                    k = BLOCKS * b + n
                    dve.wait_ge(e_done, k + 1)
                    for c in range(CHUNKS):
                        at = n * CHUNKS + c
                        if static:
                            dve.wait_ge(adj_transposed, CHUNKS * k + c + 1)
                        else:
                            dve.wait_ge(adj_transposed, counts[at % 2])
                            dve.reg_add(counts[(at + 1) % 2], counts[at % 2], 1)
                        chunk = block[:, n % BLOCK_BUFS, c * CHUNK:(c + 1) * CHUNK]
                        dve.tensor_tensor_reduce(chunk, at_ps[:, at_bank[at], :], chunk, 1.0, NEG_BIG,
                                                 ALU.mult, ALU.max, chunk_max[:, n % 2, c:c + 1]
                                                 ).then_inc(s_done, 1)
                        if c == 0 and not (first and n == 0):
                            invert((n - 1) % BLOCKS, k - 1)
                    side(n - 1, 1)
                    dve.wait_ge(s_done, CHUNKS * (k + 1))
                    wait(dve, exp_done, k - 1)
                    dve.tensor_reduce(neg_max[:, n % 2, :], chunk_max[:, n % 2, :], AX_X, ALU.max,
                                      negate=True).then_inc(max_done, 1)
                    if not (last and n == BLOCKS - 1):
                        leaky((n + 1) % BLOCKS, k + 1)
                    side(n, 0)

            batches(dve, body)
            invert(BLOCKS - 1, B * BLOCKS - 1)
            for c in range(CHUNKS // 2, CHUNKS):
                dve.wait_ge(mm_done, CHUNKS * (BLOCKS * B - 1) + c + 1)
                dve.tensor_copy(yT_sb[:, c * CHUNK:(c + 1) * CHUNK], yT_ps[:, c, :]).then_inc(yT_copied, 1)
            for q in range(CHUNKS):
                add_residual(B - 1, q, side_base(B) + q + 1)

        @code.tensor
        def _(pe):
            def transpose_chunk(b, n, c):
                m, half = n // PER_UNIT, n % PER_UNIT
                at = n * CHUNKS + c
                if c == 0 and half == 0:
                    pe.wait_ge(adj_landed[m % UNIT_BUFS], 16 * (UNITS // UNIT_BUFS * b + m // UNIT_BUFS + 1))
                wait(pe, s_done, AT_PER_BATCH * b + chunk_before(at) + 1)
                for r in range(PER_CHUNK):
                    last = pe.transpose(at_ps[:, at_bank[at], r * P:(r + 1) * P],
                                        adj_sb[:, m % UNIT_BUFS, c * PER_CHUNK + r, half * P:(half + 1) * P],
                                        ident[:])
                last.then_inc(adj_transposed, 1)

            def multiply_chunk(b, n, c):
                count = BLOCKS * b + n
                if c == 0:
                    pe.wait_ge(xn_done, count + 1)
                if n == 0:
                    wait(pe, yT_copied, CHUNKS * b)
                pe.matmul(yT_ps[:, c, :], xn[:, n % 2, :], block[:, n % BLOCK_BUFS, c * CHUNK:(c + 1) * CHUNK],
                          start=(n == 0), stop=(n == BLOCKS - 1)).then_inc(mm_done, 1)

            def side_piece(b, kind, part, count):
                wait(pe, side_drained, count - 1)
                if kind == "F":
                    pe.wait_ge(dots_done, dots_before(b))
                    pe.transpose(side_ps[0:BLOCKS, 0:P], f_new[:, 0, :], ident[:]).then_inc(side_made, 1)
                else:
                    if part == 0:
                        pe.wait_ge(yT_copied, CHUNKS * (b + 1))
                    for i in range(PER_CHUNK):
                        r = part * PER_CHUNK + i
                        last = pe.matmul(side_ps[:, i * P:(i + 1) * P], yT_sb[:, r * P:(r + 1) * P], w_sb[:],
                                         start=True, stop=True)
                    last.then_inc(side_made, 1)

            pe.wait_ge(ident_ready, 1)
            pe.wait_ge(weights_landed, 48)
            pe.transpose(side_ps[:, 0:P], w_sb[:], ident[:]).then_inc(wT_made, 1)
            pe.wait_ge(wT_copied, 1)
            for kind in range(2):
                pe.matmul(at_ps[:, kind, 0:F], a12[:, kind:kind + 1].broadcast_to([P, P]), wT[:],
                          start=True, stop=True).then_inc(wa_made, 1)
            for q in range(CHUNKS):
                pe.wait_ge(first_f1, PER_CHUNK * (q + 1))
                for i in range(PER_CHUNK):
                    r = q * PER_CHUNK + i
                    last = pe.transpose(yT_ps[:, q, i * P:(i + 1) * P], f_new[:, 0, r:r + 1].broadcast_to([P, P]),
                                        ident[:])
                last.then_inc(first_made, 1)
            pe.wait_ge(wa_ready, 2)
            for c in range(AT_BANKS):
                transpose_chunk(0, 0, c)
            for engine in range(2):
                pe.wait_ge(first_drained[engine], CHUNKS // 2)

            def body(b, first, last):
                todo = [(step, place, kind, part, i) for i, (step, place, kind, part)
                        in enumerate(pieces(first, last))]

                def side(step, place):
                    for s, p, kind, part, i in todo:
                        if (s, p) == (step, place):
                            side_piece(b - 1 if kind == "O" else b + 1, kind, part, side_base(b) + i + 1)

                for n in range(BLOCKS):
                    transpose_chunk(b, n, CHUNKS - 1)
                    for c in range(CHUNKS):
                        if n > 0:
                            multiply_chunk(b, n - 1, c)
                        elif not first:
                            multiply_chunk(b - 1, BLOCKS - 1, c)
                        if c < CHUNKS - 1:
                            if n + 1 < BLOCKS:
                                transpose_chunk(b, n + 1, c)
                            elif not last:
                                transpose_chunk(b + 1, 0, c)
                        if c == 1:
                            side(n, 0)
                    side(n, 1)

            batches(pe, body)
            for c in range(CHUNKS):
                multiply_chunk(B - 1, BLOCKS - 1, c)
            for q in range(CHUNKS):
                side_piece(B - 1, "O", q, side_base(B) + q + 1)


_INS = ["x", "adj", "L0_gnn_W", "L0_gnn_a1", "L0_gnn_a2", "L0_gnn_bias"]


def kernel(**inputs):
    import numpy as _np
    import concourse.bacc as _bacc
    from concourse import mybir as _mybir
    from concourse.bass_utils import run_bass_kernel_spmd as _run

    nc = _bacc.Bacc("TRN2", target_bir_lowering=False, num_devices=1)
    arrays, args = {}, []
    for name in _INS:
        a = _np.ascontiguousarray(inputs[name])
        arrays[f"in_{name}_dram"] = a
        args.append(nc.dram_tensor(f"in_{name}_dram", a.shape, _mybir.dt.from_np(a.dtype), kind="ExternalInput").ap())
    args.append(nc.dram_tensor("out_0_dram", tuple(inputs["x"].shape), F32, kind="ExternalOutput").ap())
    gat_kernel(nc, *args)
    r = _run(nc, [arrays], core_ids=[0])
    return r.results[0]["out_0_dram"]
```

```python
from contextlib import ExitStack

import concourse.bass as bass
from concourse import mybir

ALU = mybir.AluOpType
ACT = mybir.ActivationFunctionType
AX_X = mybir.AxisListType.X
F32 = mybir.dt.float32
F32R = mybir.dt.float32r

P = 128
CHUNK = 512
SLOPE = 0.2
NEG_BIG = -3.4028234663852886e38

AT_BANKS = 3
BLOCK_BUFS = 4
UNIT_COLS = 256
UNIT_BUFS = 4


def gat_kernel(
    nc: bass.Bass,
    x: bass.AP,
    adj: bass.AP,
    W: bass.AP,
    a1: bass.AP,
    a2: bass.AP,
    bias: bass.AP,
    out: bass.AP,
):
    B, N, F = x.shape
    O = W.shape[1]
    assert F == P and O == P and N % CHUNK == 0
    BLOCKS = N // P
    CHUNKS = N // CHUNK
    PER_CHUNK = CHUNK // P
    AT_PER_BATCH = BLOCKS * CHUNKS
    UNITS = N // UNIT_COLS
    PER_UNIT = UNIT_COLS // P
    assert UNITS % UNIT_BUFS == 0 and BLOCKS % BLOCK_BUFS == 0

    at_bank = [i % AT_BANKS for i in range(AT_PER_BATCH)]

    def chunk_before(i):
        j = i - 1
        while at_bank[j % AT_PER_BATCH] != at_bank[i]:
            j -= 1
        return j

    O_PIECES = [(1 + q // 2, q % 2, "O", q) for q in range(CHUNKS)]
    F_PIECES = [(10, 1, "F", 0)]
    PER_BODY = len(O_PIECES) + len(F_PIECES)
    SPLIT = 1
    FIRST_SPLIT = CHUNKS - SPLIT
    DOTS = [(kind, q) for q in range(CHUNKS) for kind in range(2)]
    FOLDS = 2
    DOT_STEPS = list(range(len(DOTS)))
    SUM_STEP = 9
    COPY_F2_STEP = 10
    ADD_STEPS = [10, 11, 12, 13]
    assert len(DOTS) == len(DOT_STEPS) and CHUNKS == len(ADD_STEPS)
    assert SUM_STEP < F_PIECES[0][0] and F_PIECES[-1][0] + 2 < BLOCKS

    def pieces(first, last):
        found = ([] if first else O_PIECES) + ([] if last else F_PIECES)
        return sorted(found)

    def side_base(b):
        if isinstance(b, int) and b == 0:
            return 0
        if isinstance(b, int) and b == B:
            return PER_BODY * (b - 1)
        return PER_BODY * b - len(O_PIECES)

    HALVES = [slice(0, BLOCKS // 2), slice(BLOCKS // 2, BLOCKS)]

    adj_units = adj.rearrange("b (t p) (u c) -> b u p t c", p=P, c=UNIT_COLS)
    x_rows = x.rearrange("b (t p) f -> b p t f", p=P)
    out_rows = out.rearrange("b (t p) f -> b p t f", p=P)
    bias_rows = bias.rearrange("(t p) f -> p t f", p=P)

    f1_dram = nc.dram_tensor("f1_dram", [BLOCKS, P], F32).ap()

    with ExitStack() as ctx:
        def sb(name, shape, dtype=F32):
            return ctx.enter_context(nc.sbuf_tensor(name, shape, dtype))

        def psum(name, shape):
            return ctx.enter_context(nc.psum_tensor(name, shape, F32))

        def sem(name):
            return ctx.enter_context(nc.semaphore(name))

        adj_sb = sb("adj_sb", [P, UNIT_BUFS, BLOCKS, UNIT_COLS])
        block = sb("block", [P, BLOCK_BUFS, N])
        f1_all = sb("f1_all", [P, 2, N])
        f1_rows = sb("f1_rows", [BLOCKS, P])
        f_new = sb("f_new", [P, 2, BLOCKS])
        f2_all = sb("f2_all", [P, 2, BLOCKS])
        x_in = sb("x_in", [P, 2, BLOCKS, F])
        products = sb("products", [P, 2, BLOCKS, F])
        bias_sb = sb("bias_sb", [P, BLOCKS, F])
        yT_sb = sb("yT_sb", [P, N])
        out_sb = sb("out_sb", [P, BLOCKS, O])
        xn = sb("xn", [P, 2, F])
        E_hi = sb("E_hi", [P, 2, SPLIT, CHUNK], F32R)
        E_lo = sb("E_lo", [P, 2, SPLIT, CHUNK], F32R)
        xn_hi = sb("xn_hi", [P, 2, F], F32R)
        xn_lo = sb("xn_lo", [P, 2, F], F32R)
        chunk_max = sb("chunk_max", [P, 2, CHUNKS])
        neg_max = sb("neg_max", [P, 2, 1])
        z_sum = sb("z_sum", [P, 2, 1])
        z_inv = sb("z_inv", [P, 2, 1])
        ident = sb("ident", [P, P])
        w_sb = sb("w_sb", [P, O])
        wa_rows = sb("wa_rows", [P, 2, F])
        wT = sb("wT", [P, P])
        a12 = sb("a12", [P, 2])

        yT_ps = psum("yT_ps", [P, CHUNKS, CHUNK])
        at_ps = psum("at_ps", [P, AT_BANKS, CHUNK])
        side_ps = psum("side_ps", [P, CHUNK])

        weights_landed = sem("weights_landed")
        bias_landed = sem("bias_landed")
        x_landed = sem("x_landed")
        x_added = sem("x_added")
        first_f2 = sem("first_f2")
        multiplied = sem("multiplied")
        dots_done = sem("dots_done")
        first_f1 = sem("first_f1")
        f1_stored = sem("f1_stored")
        f1_spread = sem("f1_spread")
        f2_copied = sem("f2_copied")
        adj_landed = [sem(f"adj_landed{i}") for i in range(UNIT_BUFS)]
        zeroed = sem("zeroed")
        ident_ready = sem("ident_ready")
        wT_made = sem("wT_made")
        wT_copied = sem("wT_copied")
        wa_made = sem("wa_made")
        wa_ready = sem("wa_ready")
        adj_transposed = sem("adj_transposed")
        t_done = sem("t_done")
        e_done = sem("e_done")
        s_done = sem("s_done")
        max_done = sem("max_done")
        exp_done = sem("exp_done")
        inv_done = sem("inv_done")
        xn_done = sem("xn_done")
        hi_done = sem("hi_done")
        lo_done = sem("lo_done")
        xn_hi_done = sem("xn_hi_done")
        xn_lo_done = sem("xn_lo_done")
        mm_done = sem("mm_done")
        yT_copied = sem("yT_copied")
        last_copied = sem("last_copied")
        first_made = sem("first_made")
        first_drained = sem("first_drained")
        side_made = sem("side_made")
        side_drained = sem("side_drained")
        out_stored = sem("out_stored")

        code = ctx.enter_context(nc.Block())

        def batches(eng, body):
            body(0, True, False)
            with eng.Fori(1, B - 1) as b:
                body(b, False, False)
            body(B - 1, False, True)

        def wait(eng, s, value):
            if not isinstance(value, int) or value > 0:
                eng.wait_ge(s, value)

        LAST_BANKS = [at_ps[:, q, :] for q in range(AT_BANKS)] + [side_ps[:]]
        assert len(LAST_BANKS) == CHUNKS

        def parity(b):
            return b % 2

        def quarter(q):
            return slice(q * PER_CHUNK, (q + 1) * PER_CHUNK)

        @code.sync
        def _(sp):
            sp.dma_start(w_sb[:], W).then_inc(weights_landed, 16)
            sp.dma_start(a12[:, 0:1], a1).then_inc(weights_landed, 16)
            sp.dma_start(a12[:, 1:2], a2).then_inc(weights_landed, 16)
            for half in HALVES:
                sp.dma_start(x_in[:, 0, half], x_rows[0, :, half]).then_inc(x_landed, 16)

            def load_adj(b, m, wait_for):
                if wait_for is not None:
                    sp.wait_ge(adj_transposed, wait_for)
                sp.dma_start(adj_sb[:, m % UNIT_BUFS], adj_units[b, m]).then_inc(
                    adj_landed[m % UNIT_BUFS], 16)

            def load_x(b, first):
                if first:
                    sp.wait_ge(first_f1, 1)
                else:
                    sp.wait_ge(xn_hi_done, BLOCKS * (b - 1))
                for half in HALVES:
                    sp.dma_start(x_in[:, parity(b), half], x_rows[b, :, half]).then_inc(x_landed, 16)

            def store_out(b):
                sp.wait_ge(side_drained, side_base(b + 1) + len(O_PIECES))
                sp.dma_start(out_rows[b], out_sb[:]).then_inc(out_stored, 16)

            def spread_f1(b):
                sp.wait_ge(side_drained, side_base(b))
                sp.dma_start(f1_dram, f1_rows[:]).then_inc(f1_stored, 16)
                sp.wait_ge(f1_stored, 16 * b)
                sp.dma_start(f1_all[:, parity(b), :].rearrange("p (o i) -> p o i", o=1),
                             f1_dram.rearrange("(o t) p -> o (t p)", o=1).partition_broadcast(P)).then_inc(f1_spread, 16)

            per_unit = PER_UNIT * CHUNKS

            def load_batch(b, first, last):
                for m in range(UNITS):
                    count = b * UNITS + m - UNIT_BUFS + 1
                    if not first and m == 6:
                        store_out(b - 1)
                    if not first and m == 1:
                        spread_f1(b)
                    load_adj(b, m, None if first and m < UNIT_BUFS else count * per_unit)
                    if first and m == UNIT_BUFS:
                        for half in HALVES:
                            sp.dma_start(bias_sb[:, half], bias_rows[:, half]).then_inc(bias_landed, 16)
                    if not last and m == (1 if first else 2):
                        load_x(b + 1, first)

            batches(sp, load_batch)
            for q in range(CHUNKS):
                sp.wait_ge(side_drained, side_base(B) + q + 1)
                rows = slice(q * PER_CHUNK, (q + 1) * PER_CHUNK)
                sp.dma_start(out_rows[B - 1, :, rows], out_sb[:, rows]).then_inc(out_stored, 16)
            sp.wait_ge(out_stored, 16 * (B - 1 + CHUNKS))

        @code.gpsimd
        def _(pool):
            pool.memset(ident[:], 0.0).then_inc(zeroed, 1)
            pool.wait_ge(zeroed, 1)
            pool.affine_select(out=ident[:], in_=ident[:], compare_op=ALU.not_equal, fill=1.0, base=0,
                               pattern=[[-1, P]], channel_multiplier=1).then_inc(ident_ready, 1)

            def multiply(b, kind, q):
                if (kind, q) == DOTS[0]:
                    pool.wait_ge(x_landed, 32 * (b + 1))
                wa = wa_rows[:, kind:kind + 1, :].broadcast_to([P, PER_CHUNK, F])
                pool.tensor_tensor(products[:, kind, quarter(q), :], x_in[:, parity(b), quarter(q), :], wa,
                                   ALU.mult).then_inc(multiplied, 1)

            def fold(b, i):
                kind, q = DOTS[i]
                width = F
                for step in range(FOLDS):
                    width //= 2
                    low = products[:, kind, quarter(q), 0:width]
                    pool.wait_ge(multiplied, (len(DOTS) * (b - 1) + i) * (FOLDS + 1) + step + 1)
                    pool.tensor_tensor(low, low, products[:, kind, quarter(q), width:2 * width], ALU.add
                                       ).then_inc(multiplied, 1)

            def copy_f2(b):
                pool.wait_ge(dots_done, b)
                pool.tensor_copy(f2_all[:, parity(b), :], f_new[:, 1, :]).then_inc(f2_copied, 1)

            def add_bias(b, q):
                pool.tensor_tensor(out_sb[:, quarter(q), :], x_in[:, parity(b), quarter(q), :],
                                   bias_sb[:, quarter(q), :], ALU.add).then_inc(x_added, 1)

            def split(b, n, k):
                pool.tensor_tensor(xn_hi[:, n % 2, :], x_in[:, parity(b), n, :],
                                   z_inv[:, n % 2, :].broadcast_to([P, F]), ALU.mult).then_inc(xn_hi_done, 1)
                pool.wait_ge(xn_hi_done, k + 1)
                pool.wait_ge(xn_done, k + 1)
                pool.tensor_tensor(xn_lo[:, n % 2, :], xn[:, n % 2, :], xn_hi[:, n % 2, :].bitcast(F32),
                                   ALU.subtract).then_inc(xn_lo_done, 1)
                for i in range(SPLIT):
                    pool.wait_ge(hi_done, SPLIT * k + i + 1)
                    c = FIRST_SPLIT + i
                    pool.tensor_tensor(E_lo[:, n % 2, i, :], block[:, n % BLOCK_BUFS, c * CHUNK:(c + 1) * CHUNK],
                                       E_hi[:, n % 2, i, :].bitcast(F32), ALU.subtract).then_inc(lo_done, 1)

            pool.wait_ge(first_f1, BLOCKS)
            pool.wait_ge(first_f2, BLOCKS)

            def body(b, first, last):
                for n in range(BLOCKS):
                    k = BLOCKS * b + n
                    if n == ADD_STEPS[0]:
                        wait(pool, out_stored, 16 * b)
                        if first:
                            pool.wait_ge(bias_landed, 32)
                    pool.wait_ge(inv_done, k + 1)
                    wait(pool, mm_done, CHUNKS * (k - 1))
                    pool.tensor_tensor(xn[:, n % 2, :], x_in[:, parity(b), n, :],
                                       z_inv[:, n % 2, :].broadcast_to([P, F]), ALU.mult).then_inc(xn_done, 1)
                    split(b, n, k)
                    if not last:
                        for i, step in enumerate(DOT_STEPS):
                            if n == step:
                                multiply(b + 1, *DOTS[i])
                                fold(b + 1, i)
                        if n == COPY_F2_STEP:
                            copy_f2(b + 1)
                    if n in ADD_STEPS:
                        add_bias(b, ADD_STEPS.index(n))

            batches(pool, body)

        @code.scalar
        def _(act):
            def take_f1(count):
                act.wait_ge(side_made, count)
                act.copy(f1_rows[:], side_ps[0:BLOCKS, 0:P]).then_inc(side_drained, 1)

            def add_f(b, n, count):
                wait(act, mm_done, CHUNKS * (count - BLOCK_BUFS + 1))
                act.activation(block[:, n % BLOCK_BUFS, :], f1_all[:, parity(b), :], ACT.Identity,
                               bias=f2_all[:, parity(b), n:n + 1], scale=1.0).then_inc(t_done, 1)

            act.wait_ge(wT_made, 1)
            act.copy(wT[:], side_ps[:, 0:P]).then_inc(wT_copied, 1)
            for kind in range(2):
                act.wait_ge(wa_made, kind + 1)
                act.copy(wa_rows[:, kind, :], at_ps[:, kind, 0:F]).then_inc(wa_ready, 1)
            for q in range(CHUNKS):
                act.wait_ge(first_made, q + 1)
                act.copy(f1_all[:, 0, q * CHUNK:(q + 1) * CHUNK], yT_ps[:, q, :]).then_inc(first_drained, 1)
            act.wait_ge(first_drained, CHUNKS)
            act.wait_ge(first_f2, 1)
            add_f(0, 0, 0)
            act.wait_ge(first_f2, BLOCKS)
            add_f(0, 1, 1)

            def body(b, first, last):
                todo = [(step, place, kind, part, i) for i, (step, place, kind, part)
                        in enumerate(pieces(first, last))]

                def side(step, place):
                    for s, p, kind, part, i in todo:
                        if (s, p) == (step, place) and kind == "F":
                            take_f1(side_base(b) + i + 1)

                for n in range(BLOCKS):
                    k = BLOCKS * b + n
                    side(n - 1, 1)
                    if n + 2 < BLOCKS:
                        add_f(b, n + 2, k + 2)
                    elif not last:
                        if n + 2 == BLOCKS:
                            act.wait_ge(f1_spread, 16 * (b + 1))
                            act.wait_ge(f2_copied, b + 1)
                        add_f(b + 1, n + 2 - BLOCKS, k + 2)
                    act.wait_ge(max_done, k + 1)
                    wait(act, inv_done, k - 1)
                    E = block[:, n % BLOCK_BUFS, :]
                    act.activation(E, E, ACT.Exp, bias=neg_max[:, n % 2, :], scale=1.0,
                                   accum_out=z_sum[:, n % 2, :]).then_inc(exp_done, 1)
                    act.wait_ge(exp_done, k + 1)
                    for i in range(SPLIT):
                        c = FIRST_SPLIT + i
                        act.copy(E_hi[:, n % 2, i, :], E[:, c * CHUNK:(c + 1) * CHUNK]).then_inc(hi_done, 1)
                    side(n, 0)
                    if n == 0 and not first:
                        copy_yT(b - 1, CHUNKS)

            def copy_yT(b, chunks):
                for c in range(chunks):
                    act.wait_ge(mm_done, CHUNKS * (BLOCKS * b + BLOCKS - 1) + c + 1)
                    act.copy(yT_sb[:, c * CHUNK:(c + 1) * CHUNK], yT_ps[:, c, :]).then_inc(yT_copied, 1)

            batches(act, body)
            copy_yT(B - 1, CHUNKS // 2)

        @code.vector
        def _(dve):
            def leaky(n, count, cols):
                dve.wait_ge(t_done, count + 1)
                t = block[:, n % BLOCK_BUFS, cols]
                dve.scalar_tensor_tensor(out=t, in0=t, scalar=SLOPE, in1=t, op0=ALU.mult,
                                         op1=ALU.max).then_inc(e_done, 1)

            def add_residual(b, part, count, bank):
                dve.wait_ge(side_made, count)
                dve.wait_ge(x_added, CHUNKS * b + part + 1)
                rows = out_sb[:, quarter(part), :]
                dve.tensor_tensor(rows, bank.rearrange("p (r o) -> p r o", o=O), rows, ALU.add
                                  ).then_inc(side_drained, 1)

            def sum_dots(b):
                dve.wait_ge(multiplied, len(DOTS) * (FOLDS + 1) * b)
                if isinstance(b, int) and b == 1:
                    dve.wait_ge(first_made, CHUNKS)
                else:
                    dve.wait_ge(side_made, side_base(b - 1))
                    dve.wait_ge(f2_copied, b - 1)
                dve.tensor_reduce(f_new[:], products[:, :, :, 0:F >> FOLDS], AX_X, ALU.add
                                  ).then_inc(dots_done, 1)

            def invert(n, count):
                dve.wait_ge(exp_done, count + 1)
                wait(dve, xn_hi_done, count - 1)
                dve.reciprocal(z_inv[:, n % 2, :], z_sum[:, n % 2, :]).then_inc(inv_done, 1)

            FIRST_COLS, OTHER_COLS = slice(0, CHUNK), slice(CHUNK, N)

            counts = [dve.alloc_register(f"chunk_count{i}") for i in range(2)]
            dve.reg_mov(counts[0], AT_PER_BATCH + 1)

            dve.wait_ge(wa_ready, 2)
            dve.wait_ge(x_landed, 32)
            for kind, to, made in ((0, f_new[:, 0, :], first_f1), (1, f2_all[:, 0, :], first_f2)):
                for r in range(BLOCKS):
                    dve.tensor_tensor_reduce(products[:, kind, r, :], x_in[:, 0, r, :], wa_rows[:, kind, :], 1.0,
                                             0.0, ALU.mult, ALU.add, to[:, r:r + 1]).then_inc(made, 1)
            leaky(0, 0, FIRST_COLS)
            leaky(0, 0, OTHER_COLS)

            def body(b, first, last):
                todo = [(step, place, kind, part, i) for i, (step, place, kind, part)
                        in enumerate(pieces(first, last))]

                def side(step, place):
                    for s, p, kind, part, i in todo:
                        if (s, p) == (step, place) and kind == "O":
                            add_residual(b - 1, part, side_base(b) + i + 1, side_ps[:])

                static = first or last
                for n in range(BLOCKS):
                    k = BLOCKS * b + n
                    for c in range(CHUNKS):
                        at = n * CHUNKS + c
                        if c < 2:
                            dve.wait_ge(e_done, 2 * k + c + 1)
                        if static:
                            dve.wait_ge(adj_transposed, CHUNKS * k + c + 1)
                        else:
                            dve.wait_ge(adj_transposed, counts[at % 2])
                            dve.reg_add(counts[(at + 1) % 2], counts[at % 2], 1)
                        chunk = block[:, n % BLOCK_BUFS, c * CHUNK:(c + 1) * CHUNK]
                        dve.tensor_tensor_reduce(chunk, at_ps[:, at_bank[at], :], chunk, 1.0, NEG_BIG,
                                                 ALU.mult, ALU.max, chunk_max[:, n % 2, c:c + 1]
                                                 ).then_inc(s_done, 1)
                        if c == 0 and not (first and n == 0):
                            invert((n - 1) % BLOCKS, k - 1)
                    side(n - 1, 1)
                    if n == SUM_STEP and not last:
                        sum_dots(b + 1)
                    more = not (last and n == BLOCKS - 1)
                    if more:
                        leaky((n + 1) % BLOCKS, k + 1, FIRST_COLS)
                    dve.wait_ge(s_done, CHUNKS * (k + 1))
                    wait(dve, exp_done, k - 1)
                    dve.tensor_reduce(neg_max[:, n % 2, :], chunk_max[:, n % 2, :], AX_X, ALU.max,
                                      negate=True).then_inc(max_done, 1)
                    if more:
                        leaky((n + 1) % BLOCKS, k + 1, OTHER_COLS)
                    side(n, 0)

            batches(dve, body)
            invert(BLOCKS - 1, B * BLOCKS - 1)
            for c in range(CHUNKS // 2, CHUNKS):
                dve.wait_ge(mm_done, CHUNKS * (BLOCKS * B - 1) + c + 1)
                dve.tensor_copy(yT_sb[:, c * CHUNK:(c + 1) * CHUNK], yT_ps[:, c, :]).then_inc(last_copied, 1)
            for q in range(CHUNKS):
                add_residual(B - 1, q, side_base(B) + q + 1, LAST_BANKS[q])

        @code.tensor
        def _(pe):
            def transpose_chunk(b, n, c):
                m, half = n // PER_UNIT, n % PER_UNIT
                at = n * CHUNKS + c
                if c == 0 and half == 0:
                    pe.wait_ge(adj_landed[m % UNIT_BUFS], 16 * (UNITS // UNIT_BUFS * b + m // UNIT_BUFS + 1))
                wait(pe, s_done, AT_PER_BATCH * b + chunk_before(at) + 1)
                for r in range(PER_CHUNK):
                    last = pe.transpose(at_ps[:, at_bank[at], r * P:(r + 1) * P],
                                        adj_sb[:, m % UNIT_BUFS, c * PER_CHUNK + r, half * P:(half + 1) * P],
                                        ident[:])
                last.then_inc(adj_transposed, 1)

            def multiply_chunk(b, n, c):
                count = BLOCKS * b + n
                if c == 0:
                    pe.wait_ge(xn_done, count + 1)
                if n == 0:
                    wait(pe, yT_copied, CHUNKS * (b - 1) + c + 1)
                if c < FIRST_SPLIT:
                    pe.matmul(yT_ps[:, c, :], xn[:, n % 2, :], block[:, n % BLOCK_BUFS, c * CHUNK:(c + 1) * CHUNK],
                              start=(n == 0), stop=(n == BLOCKS - 1)).then_inc(mm_done, 1)
                    return
                i = c - FIRST_SPLIT
                pe.wait_ge(xn_hi_done, count + 1)
                pe.wait_ge(hi_done, SPLIT * count + i + 1)
                pe.matmul(yT_ps[:, c, :], xn_hi[:, n % 2, :], E_hi[:, n % 2, i, :], start=(n == 0), stop=False)
                pe.wait_ge(xn_lo_done, count + 1)
                pe.matmul(yT_ps[:, c, :], xn_lo[:, n % 2, :], E_hi[:, n % 2, i, :], start=False, stop=False)
                pe.wait_ge(lo_done, SPLIT * count + i + 1)
                pe.matmul(yT_ps[:, c, :], xn_hi[:, n % 2, :], E_lo[:, n % 2, i, :], start=False,
                          stop=(n == BLOCKS - 1)).then_inc(mm_done, 1)

            def side_piece(b, kind, part, count):
                wait(pe, side_drained, count - 1)
                if kind == "F":
                    pe.wait_ge(dots_done, b)
                    pe.transpose(side_ps[0:BLOCKS, 0:P], f_new[:, 0, :], ident[:]).then_inc(side_made, 1)
                else:
                    pe.wait_ge(yT_copied, CHUNKS * b + part + 1)
                    multiply_W(part, side_ps).then_inc(side_made, 1)

            def multiply_W(part, bank):
                for i in range(PER_CHUNK):
                    r = part * PER_CHUNK + i
                    last = pe.matmul(bank[:, i * P:(i + 1) * P], yT_sb[:, r * P:(r + 1) * P], w_sb[:],
                                     start=True, stop=True)
                return last

            pe.wait_ge(ident_ready, 1)
            pe.wait_ge(weights_landed, 48)
            pe.transpose(side_ps[:, 0:P], w_sb[:], ident[:]).then_inc(wT_made, 1)
            pe.wait_ge(wT_copied, 1)
            for kind in range(2):
                pe.matmul(at_ps[:, kind, 0:F], a12[:, kind:kind + 1].broadcast_to([P, P]), wT[:],
                          start=True, stop=True).then_inc(wa_made, 1)
            for q in range(CHUNKS):
                pe.wait_ge(first_f1, PER_CHUNK * (q + 1))
                for i in range(PER_CHUNK):
                    r = q * PER_CHUNK + i
                    last = pe.transpose(yT_ps[:, q, i * P:(i + 1) * P], f_new[:, 0, r:r + 1].broadcast_to([P, P]),
                                        ident[:])
                last.then_inc(first_made, 1)
            pe.wait_ge(wa_ready, 2)
            for c in range(AT_BANKS):
                transpose_chunk(0, 0, c)
            pe.wait_ge(first_drained, CHUNKS)

            def body(b, first, last):
                todo = [(step, place, kind, part, i) for i, (step, place, kind, part)
                        in enumerate(pieces(first, last))]

                def side(step, place):
                    for s, p, kind, part, i in todo:
                        if (s, p) == (step, place):
                            side_piece(b - 1 if kind == "O" else b + 1, kind, part, side_base(b) + i + 1)

                for n in range(BLOCKS):
                    transpose_chunk(b, n, CHUNKS - 1)
                    for c in range(CHUNKS):
                        if n > 0:
                            multiply_chunk(b, n - 1, c)
                        elif not first:
                            multiply_chunk(b - 1, BLOCKS - 1, c)
                        if c < CHUNKS - 1:
                            if n + 1 < BLOCKS:
                                transpose_chunk(b, n + 1, c)
                            elif not last:
                                transpose_chunk(b + 1, 0, c)
                        if c == 1:
                            side(n, 0)
                    side(n, 1)

            batches(pe, body)
            for c in range(CHUNKS):
                multiply_chunk(B - 1, BLOCKS - 1, c)
            for q in range(CHUNKS):
                if q < CHUNKS // 2:
                    pe.wait_ge(yT_copied, CHUNKS * (B - 1) + q + 1)
                else:
                    pe.wait_ge(last_copied, q - CHUNKS // 2 + 1)
                multiply_W(q, LAST_BANKS[q]).then_inc(side_made, 1)


_INS = ["x", "adj", "L0_gnn_W", "L0_gnn_a1", "L0_gnn_a2", "L0_gnn_bias"]


def kernel(**inputs):
    import numpy as _np
    import concourse.bacc as _bacc
    from concourse import mybir as _mybir
    from concourse.bass_utils import run_bass_kernel_spmd as _run

    nc = _bacc.Bacc("TRN2", target_bir_lowering=False, num_devices=1)
    arrays, args = {}, []
    for name in _INS:
        a = _np.ascontiguousarray(inputs[name])
        arrays[f"in_{name}_dram"] = a
        args.append(nc.dram_tensor(f"in_{name}_dram", a.shape, _mybir.dt.from_np(a.dtype), kind="ExternalInput").ap())
    args.append(nc.dram_tensor("out_0_dram", tuple(inputs["x"].shape), F32, kind="ExternalOutput").ap())
    gat_kernel(nc, *args)
    r = _run(nc, [arrays], core_ids=[0])
    return r.results[0]["out_0_dram"]
```
